# Optimizing a Trainium2 kernel written in Bass

```python
import numpy as np
import jax
import jax.numpy as jnp

def _softmax(x, axis=-1):
    return jax.nn.softmax(x, axis=axis)

def _gelu(x):
    return jax.nn.gelu(x, approximate=True)

def _silu(x):
    return jax.nn.silu(x)

def _sigmoid(x):
    return jax.nn.sigmoid(x)

def _layernorm(x, axis=-1, eps=1e-05):
    m = jnp.mean(x, axis=axis, keepdims=True)
    v = jnp.var(x, axis=axis, keepdims=True)
    return (x - m) / jnp.sqrt(v + eps)

def _scatter_add(tgt, idx, src, axis=0):
    return tgt.at[idx].add(src)

def _segment_sum(src, seg, n):
    return jax.ops.segment_sum(src, seg, n)
kernel_name = 'mk_adaln_ffn_d1_seqx_r8_79a960'

def setup_inputs(seed: int=0):
    np.random.seed(seed)
    _w = jnp.asarray

    def _rec_inputs():
        import jax
        import jax.numpy as jnp
        _rk = jax.random.key(seed)
        x = -7.109e-05 + 0.9999 * jax.random.normal(jax.random.fold_in(_rk, 1), (64, 32, 512), jnp.float32)
        _lenS = 32 - jax.random.randint(jax.random.fold_in(_rk, 7), (64,), 0, max(1, 32 // 4) + 1, jnp.int32)
        _lenS2 = 32 - jax.random.randint(jax.random.fold_in(_rk, 8), (64,), 0, max(1, 32 // 4) + 1, jnp.int32)
        itok_B_0_15 = jax.random.randint(jax.random.fold_in(_rk, 11), (64,), 0, 16, jnp.int32)
        return (x, itok_B_0_15)
    x, itok_B_0_15 = _rec_inputs()

    def _L0_cond_setup():
        import jax, jax.numpy as jnp
        import numpy as np
        NUM_CONDITIONS = 16
        IN_CH = 32
        OUT_CH = 32
        B = 64
        T = 512
        key = jax.random.key(seed)
        k_x, k_w, k_c = jax.random.split(key, 3)
        x = jax.random.normal(k_x, (B, IN_CH, T), dtype=jnp.float32)
        bound = float(np.sqrt(6.0 / IN_CH))
        weights = jax.random.uniform(k_w, (NUM_CONDITIONS, IN_CH, OUT_CH), dtype=jnp.float32, minval=-bound, maxval=bound)
        condition = jax.random.randint(k_c, (B,), 0, NUM_CONDITIONS, dtype=jnp.int64)
        return {'x': x, 'weights': weights, 'condition': condition}
    _L0_cond_all = _L0_cond_setup()
    _L0_cond_in = {k: v for k, v in _L0_cond_all.items() if k in ('weights',)}
    del _L0_cond_all

    def _L0_ffn_setup():
        import jax, jax.numpy as jnp
        import numpy as np
        N_EXPERTS = 28
        TOP_K = 2
        RANK = 8
        LORA_ALPHA = 16
        SCALING = LORA_ALPHA / RANK
        TEMP = 1.0
        key = jax.random.key(seed)
        ks = jax.random.split(key, 5)
        B, S, D_IN, D_OUT = (4, 256, 512, 512)
        x = jax.random.normal(ks[0], (B, S, D_IN), dtype=jnp.float32)
        base_W = jax.random.normal(ks[1], (D_OUT, D_IN), dtype=jnp.float32) * (1.0 / np.sqrt(D_IN))
        gate_W = jax.random.normal(ks[2], (N_EXPERTS, D_IN), dtype=jnp.float32) * (1.0 / np.sqrt(D_IN))
        lora_A = jax.random.normal(ks[3], (N_EXPERTS, RANK, D_IN), dtype=jnp.float32) * (1.0 / np.sqrt(D_IN))
        lora_B = jax.random.normal(ks[4], (N_EXPERTS, D_OUT, RANK), dtype=jnp.float32) * 0.01
        return {'x': x, 'base_W': base_W, 'gate_W': gate_W, 'lora_A': lora_A, 'lora_B': lora_B}
    _L0_ffn_all = _L0_ffn_setup()
    _L0_ffn_in = {k: v for k, v in _L0_ffn_all.items() if k in ('base_W', 'gate_W', 'lora_A', 'lora_B')}
    del _L0_ffn_all
    return {'x': x, 'itok_B_0_15': itok_B_0_15, 'L0_cond_weights': _L0_cond_in['weights'], 'L0_ffn_base_W': _L0_ffn_in['base_W'], 'L0_ffn_gate_W': _L0_ffn_in['gate_W'], 'L0_ffn_lora_A': _L0_ffn_in['lora_A'], 'L0_ffn_lora_B': _L0_ffn_in['lora_B']}

def reference(x, itok_B_0_15, L0_cond_weights, L0_ffn_base_W, L0_ffn_gate_W, L0_ffn_lora_A, L0_ffn_lora_B):
    import jax
    import jax.numpy as jnp

    def _L0_cond_ref(x, weights, condition):
        import jax, jax.numpy as jnp
        import numpy as np
        NUM_CONDITIONS = 16
        IN_CH = 32
        OUT_CH = 32
        B = 64
        T = 512
        W = weights[condition]
        return jnp.einsum('bct,bcd->bdt', x, W)

    def _L0_ffn_ref(x, base_W, gate_W, lora_A, lora_B):
        import jax, jax.numpy as jnp
        import numpy as np
        N_EXPERTS = 28
        TOP_K = 2
        RANK = 8
        LORA_ALPHA = 16
        SCALING = LORA_ALPHA / RANK
        TEMP = 1.0
        B, S, D_in = x.shape
        xf = x.reshape(B * S, D_in)
        base = xf @ base_W.T
        logits = xf @ gate_W.T
        top_vals, top_idx = jax.lax.top_k(logits, TOP_K)
        top_probs = jax.nn.softmax(top_vals / TEMP, axis=-1)
        N = xf.shape[0]
        gate_full = jnp.zeros((N, N_EXPERTS), dtype=xf.dtype).at[jnp.arange(N)[:, None], top_idx].add(top_probs)
        h = jnp.einsum('nd,erd->ner', xf, lora_A)
        h = h * (gate_full * SCALING)[:, :, None]
        lora_out = jnp.einsum('ner,eor->no', h, lora_B)
        out = base + lora_out
        return out.reshape(B, S, -1)
    x = x + _L0_ffn_ref(_L0_cond_ref(x, L0_cond_weights, itok_B_0_15), L0_ffn_base_W, L0_ffn_gate_W, L0_ffn_lora_A, L0_ffn_lora_B)
    return x

_drawn_inputs = setup_inputs


def setup_inputs(seed=0):
    import zlib

    import numpy as np

    out = dict(_drawn_inputs(seed))
    spreads = {}
    factors = {}
    for name, (base, spread) in spreads.items():
        noise = np.random.default_rng([zlib.crc32(name.encode()), seed]).standard_normal(out[name].shape)
        drawn = base * np.exp(spread * noise) if base else spread * noise
        out[name] = jnp.asarray(drawn.astype(out[name].dtype))
    for name, factor in factors.items():
        out[name] = (out[name] * factor).astype(out[name].dtype)
    return out
```

```python
from contextlib import ExitStack

import concourse.bass as bass
from concourse import mybir

F32 = mybir.dt.float32
F32R = mybir.dt.float32r
I32 = mybir.dt.int32
U32 = mybir.dt.uint32
ALU = mybir.AluOpType
ACT = mybir.ActivationFunctionType

P = 128
TOP8 = 8
SCALING = 16 / 8
AHEAD = 4


def mixed_lora_ffn(nc, x, condition, mix_weights, base_wT, hl_wT, lora_b, out):
    ROWS, T = x.shape
    NUM_COND, C, _ = mix_weights.shape
    ER, D_OUT = lora_b.shape
    E = hl_wT.shape[1] - ER
    RANK = ER // E
    HL = ER + E
    BATCHES = P // C
    GROUPS = ROWS // P
    TC = T // P
    EC = 2
    EK = ER // EC
    XW = T + P
    assert GROUPS % 2 == 0 and T % P == 0 and EK <= P and HL <= 512 and D_OUT <= 512

    x_g = x.rearrange("(g p) t -> g p t", p=P)
    out_g = out.rearrange("(g p) t -> g p t", p=P)
    cond_g = condition.rearrange("(g b) -> g b", b=BATCHES)
    base_v = base_wT.rearrange("(k p) n -> p k n", p=P)
    hl_v = hl_wT.rearrange("(k p) n -> p k n", p=P)
    lora_b_v = lora_b.rearrange("(k p) n -> p k n", p=EK)

    with ExitStack() as ctx:
        def sb(name, shape, dt=F32):
            return ctx.enter_context(nc.sbuf_tensor(name, shape, dt))

        def ps(name, shape):
            return ctx.enter_context(nc.psum_tensor(name, shape, F32))

        def sem(name):
            return ctx.enter_context(nc.semaphore(name))

        xw = sb("xw", [P, GROUPS, XW])
        xw_hi = sb("xw_hi", [P, XW], F32R)
        xw_lo = sb("xw_lo", [P, XW], F32R)
        y_hi = sb("y_hi", [P, TC, P], F32R)
        y_lo = sb("y_lo", [P, TC, P], F32R)
        hl_w = sb("hl_w", [P, TC, HL])
        hl_w_hi = sb("hl_w_hi", [P, TC, HL], F32R)
        hl_w_lo = sb("hl_w_lo", [P, TC, HL], F32R)
        base_w = sb("base_w", [P, TC, D_OUT])
        base_w_hi = sb("base_w_hi", [P, TC, D_OUT], F32R)
        base_w_lo = sb("base_w_lo", [P, TC, D_OUT], F32R)
        lb = sb("lb", [P, EC, D_OUT])
        lb_hi = sb("lb_hi", [P, EC, D_OUT], F32R)
        lb_lo = sb("lb_lo", [P, EC, D_OUT], F32R)
        gated = sb("gated", [P, ER])
        gT_hi = sb("gT_hi", [P, EC, P], F32R)
        gT_lo = sb("gT_lo", [P, EC, P], F32R)
        ident = sb("ident", [P, P])
        expert_i = sb("expert_i", [P, E], I32)
        expert = sb("expert", [P, E])
        logit = sb("logit", [P, E])
        top = sb("top", [P, TOP8])
        top_at = sb("top_at", [P, TOP8], U32)
        top_atf = sb("top_atf", [P, 2])
        ratio = sb("ratio", [P, 1])
        halfsum = sb("halfsum", [P, 1])
        norm = sb("norm", [P, 1])
        second = sb("second", [P, E])
        gate = sb("gate", [P, E])
        result = sb("result", [P, 2, D_OUT])

        yT_ps = ps("yT_ps", [P, TC, P])
        hl_ps = ps("hl_ps", [P, 512])
        gT_ps = ps("gT_ps", [P, EC, 256])
        out_ps = [ps(f"out_ps{i}", [P, D_OUT]) for i in range(2)]

        h_ps = hl_ps[:, 0:ER].rearrange("p (e r) -> p e r", r=RANK)

        blocks_zeroed = sem("blocks_zeroed")
        group_loaded = [sem(f"group_loaded{i}") for i in range(2)]
        hl_w_loaded = sem("hl_w_loaded")
        base_w_loaded = [sem(f"base_w_loaded{k}") for k in range(TC)]
        lb_loaded = sem("lb_loaded")
        hl_w_hi_ready = sem("hl_w_hi_ready")
        hl_w_lo_ready = sem("hl_w_lo_ready")
        base_w_hi_ready = sem("base_w_hi_ready")
        base_w_lo_ready = sem("base_w_lo_ready")
        lb_hi_ready = sem("lb_hi_ready")
        lb_lo_ready = sem("lb_lo_ready")
        ident_zeroed = sem("ident_zeroed")
        ident_ready = sem("ident_ready")
        expert_i_ready = sem("expert_i_ready")
        expert_ready = sem("expert_ready")
        xw_hi_ready = sem("xw_hi_ready")
        xw_lo_ready = sem("xw_lo_ready")
        mixed = sem("mixed")
        y_hi_ready = sem("y_hi_ready")
        y_lo_ready = sem("y_lo_ready")
        hl_done = sem("hl_done")
        logit_ready = sem("logit_ready")
        top_ready = sem("top_ready")
        top_at_ready = sem("top_at_ready")
        top_atf_ready = sem("top_atf_ready")
        ratio_ready = sem("ratio_ready")
        halfsum_ready = sem("halfsum_ready")
        norm_ready = sem("norm_ready")
        second_ready = sem("second_ready")
        gate_ready = sem("gate_ready")
        gated_ready = sem("gated_ready")
        turned = sem("turned")
        gT_hi_ready = sem("gT_hi_ready")
        gT_lo_ready = sem("gT_lo_ready")
        out_done = sem("out_done")
        result_ready = sem("result_ready")
        stored = [sem(f"stored{i}") for i in range(2)]

        LOAD = 16 * (1 + BATCHES)
        PAIRS = (GROUPS - 2) // 2

        block = ctx.enter_context(nc.Block())

        @block.sync
        def _(sp):
            def load(half, odd):
                g = 2 * half + odd
                if not isinstance(half, int) or half > 0:
                    sp.wait_ge(group_loaded[odd], LOAD * half)
                sp.dma_start(xw[:, bass.ds(g, 1), 0:T].rearrange("p a t -> p (a t)"),
                             x_g[bass.ds(g, 1)].rearrange("a p t -> (a p) t")).then_inc(group_loaded[odd], 16)
                if isinstance(half, int) and g == 0:
                    sp.wait_ge(blocks_zeroed, 1)
                for b in range(BATCHES):
                    c = sp.value_load(cond_g[bass.ds(g, 1), b:b + 1], min_val=0, max_val=NUM_COND - 1)
                    sp.dma_start(xw[b * C:(b + 1) * C, bass.ds(g, 1), T + b * C:T + (b + 1) * C]
                                 .rearrange("p a d -> p (a d)"),
                                 mix_weights[bass.ds(c, 1)].rearrange("a c d -> (a c) d")
                                 ).then_inc(group_loaded[odd], 16)

            def store(half, odd):
                g = 2 * half + odd
                sp.wait_ge(result_ready, g + 1)
                sp.dma_start(out_g[bass.ds(g, 1)].rearrange("a p t -> (a p) t"),
                             result[:, odd, :]).then_inc(stored[odd], 16)

            for g in range(AHEAD):
                load(g // 2, g % 2)
            with sp.Fori(0, (GROUPS - AHEAD) // 2) as half:
                load(half + AHEAD // 2, 0)
                store(half, 0)
                load(half + AHEAD // 2, 1)
                store(half, 1)
            for g in range(GROUPS - AHEAD, GROUPS):
                store(g // 2, g % 2)
            for odd in range(2):
                sp.wait_ge(stored[odd], 16 * (GROUPS // 2))

        @block.gpsimd
        def _(pool):
            nc.gpsimd.memset(ident[:], 0.0).then_inc(ident_zeroed, 1)
            nc.gpsimd.iota(expert_i[:], pattern=[[1, E]], base=0, channel_multiplier=0).then_inc(expert_i_ready, 1)
            pool.wait_ge(ident_zeroed, 1)
            nc.gpsimd.affine_select(out=ident[:], in_=ident[:], compare_op=ALU.not_equal, fill=1.0, base=0,
                                    pattern=[[-1, P]], channel_multiplier=1).then_inc(ident_ready, 1)
            pool.wait_ge(expert_i_ready, 1)
            nc.gpsimd.tensor_copy(expert[:], expert_i[:]).then_inc(expert_ready, 1)

            def split_lo(g):
                pool.wait_ge(xw_hi_ready, g + 1)
                if not isinstance(g, int) or g > 0:
                    pool.wait_ge(mixed, g)
                nc.gpsimd.tensor_tensor(xw_lo[:], xw[:, bass.ds(g, 1), :].rearrange("p a t -> p (a t)"),
                                        xw_hi[:].bitcast(F32), ALU.subtract).then_inc(xw_lo_ready, 1)

            split_lo(0)
            with pool.Fori(1, GROUPS) as g:
                split_lo(g)

        @block.scalar
        def _(act):
            act.dma_start(hl_w[:], hl_v).then_inc(hl_w_loaded, 16)
            for k in range(TC):
                act.dma_start(base_w[:, k, :], base_v[:, k, :]).then_inc(base_w_loaded[k], 16)
            act.dma_start(lb[0:EK], lora_b_v).then_inc(lb_loaded, 16)

            def split_hi(half, odd):
                g = 2 * half + odd
                act.wait_ge(group_loaded[odd], LOAD * (half + 1))
                if not isinstance(g, int) or g > 0:
                    act.wait_ge(mixed, g)
                    act.wait_ge(xw_lo_ready, g)
                nc.scalar.copy(xw_hi[:], xw[:, bass.ds(g, 1), :].rearrange("p a t -> p (a t)")
                               ).then_inc(xw_hi_ready, 1)

            def mixed_hi(g):
                act.wait_ge(mixed, g + 1)
                if not isinstance(g, int) or g > 0:
                    act.wait_ge(y_lo_ready, g)
                nc.scalar.copy(y_hi[:], yT_ps[:]).then_inc(y_hi_ready, 1)

            def gate_ratio(g):
                act.wait_ge(top_ready, g + 1)
                if not isinstance(g, int) or g > 0:
                    act.wait_ge(gate_ready, g)
                    act.wait_ge(halfsum_ready, g)
                nc.scalar.activation(ratio[:], top[:, 0:1], ACT.Exp, bias=top[:, 1:2], scale=-1.0
                                     ).then_inc(ratio_ready, 1)
                act.wait_ge(top_at_ready, g + 1)
                nc.scalar.copy(top_atf[:], top_at[:, 0:2]).then_inc(top_atf_ready, 1)

            def turned_hi(g):
                act.wait_ge(turned, g + 1)
                if not isinstance(g, int) or g > 0:
                    act.wait_ge(out_done, g)
                    act.wait_ge(gT_lo_ready, g)
                nc.scalar.copy(gT_hi[0:EK], gT_ps[0:EK, :, 0:P]).then_inc(gT_hi_ready, 1)

            split_hi(0, 0)
            act.wait_ge(hl_w_loaded, 16)
            nc.scalar.copy(hl_w_hi[:], hl_w[:]).then_inc(hl_w_hi_ready, 1)
            mixed_hi(0)
            for k in range(TC):
                act.wait_ge(base_w_loaded[k], 16)
                nc.scalar.copy(base_w_hi[:, k, :], base_w[:, k, :]).then_inc(base_w_hi_ready, 1)
            split_hi(0, 1)
            gate_ratio(0)
            act.wait_ge(lb_loaded, 16)
            nc.scalar.copy(lb_hi[0:EK], lb[0:EK]).then_inc(lb_hi_ready, 1)
            mixed_hi(1)

            def pair(half):
                for odd in (0, 1):
                    g = 2 * half + 1 + odd
                    turned_hi(g - 1)
                    split_hi(half + 1, odd)
                    gate_ratio(g)
                    mixed_hi(g + 1)

            pair(0)
            with act.Fori(1, PAIRS) as half:
                pair(half)
            turned_hi(GROUPS - 2)
            gate_ratio(GROUPS - 1)
            turned_hi(GROUPS - 1)

        @block.vector
        def _(dve):
            nc.vector.memset(xw[:, :, T:XW], 0.0).then_inc(blocks_zeroed, 1)

            def mixed_lo(g):
                dve.wait_ge(y_hi_ready, g + 1)
                nc.vector.tensor_tensor(y_lo[:], yT_ps[:], y_hi[:].bitcast(F32), ALU.subtract
                                        ).then_inc(y_lo_ready, 1)

            def top_two(g):
                dve.wait_ge(hl_done, g + 1)
                nc.vector.tensor_copy(logit[:], hl_ps[:, ER:HL]).then_inc(logit_ready, 1)
                dve.wait_ge(expert_ready, 1)
                dve.wait_ge(logit_ready, g + 1)
                if not isinstance(g, int) or g > 0:
                    dve.wait_ge(ratio_ready, g)
                nc.vector.max(top[:], logit[:]).then_inc(top_ready, 1)
                dve.wait_ge(expert_ready, 1)
                dve.wait_ge(top_ready, g + 1)
                if not isinstance(g, int) or g > 0:
                    dve.wait_ge(top_atf_ready, g)
                nc.vector.max_index(top_at[:], top[:], logit[:]).then_inc(top_at_ready, 1)

            def gating(g):
                dve.wait_ge(ratio_ready, g + 1)
                nc.vector.tensor_scalar(halfsum[:], ratio[:], 1.0, 1.0 / SCALING, ALU.add, ALU.mult
                                        ).then_inc(halfsum_ready, 1)
                dve.wait_ge(top_atf_ready, g + 1)
                nc.vector.tensor_scalar(second[:], expert[:], top_atf[:, 1:2], ratio[:], ALU.is_equal, ALU.mult
                                        ).then_inc(second_ready, 1)
                dve.wait_ge(halfsum_ready, g + 1)
                nc.vector.reciprocal(norm[:], halfsum[:]).then_inc(norm_ready, 1)
                dve.wait_ge(second_ready, g + 1)
                nc.vector.scalar_tensor_tensor(gate[:], expert[:], top_atf[:, 0:1], second[:],
                                               ALU.is_equal, ALU.add).then_inc(gate_ready, 1)
                dve.wait_ge(norm_ready, g + 1)
                dve.wait_ge(gate_ready, g + 1)
                if not isinstance(g, int) or g > 0:
                    dve.wait_ge(turned, g)
                nc.vector.scalar_tensor_tensor(gated[:].rearrange("p (e r) -> p e r", r=RANK), h_ps, norm[:, 0:1],
                                               gate[:].unsqueeze(2).broadcast_to([P, E, RANK]),
                                               ALU.mult, ALU.mult).then_inc(gated_ready, 1)

            def turned_lo(g):
                dve.wait_ge(gT_hi_ready, g + 1)
                if not isinstance(g, int) or g > 0:
                    dve.wait_ge(out_done, g)
                nc.vector.tensor_tensor(gT_lo[0:EK], gT_ps[0:EK, :, 0:P], gT_hi[0:EK].bitcast(F32), ALU.subtract
                                        ).then_inc(gT_lo_ready, 1)

            def finish(half, odd):
                g = 2 * half + odd
                dve.wait_ge(out_done, g + 1)
                if not isinstance(half, int) or half > 0:
                    dve.wait_ge(stored[odd], 16 * half)
                nc.vector.tensor_tensor(result[:, odd, :], out_ps[odd][:],
                                        xw[:, bass.ds(g, 1), 0:T].rearrange("p a t -> p (a t)"), ALU.add
                                        ).then_inc(result_ready, 1)

            dve.wait_ge(hl_w_hi_ready, 1)
            nc.vector.tensor_tensor(hl_w_lo[:], hl_w[:], hl_w_hi[:].bitcast(F32), ALU.subtract
                                    ).then_inc(hl_w_lo_ready, 1)
            mixed_lo(0)
            for k in range(TC):
                dve.wait_ge(base_w_hi_ready, k + 1)
                nc.vector.tensor_tensor(base_w_lo[:, k, :], base_w[:, k, :], base_w_hi[:, k, :].bitcast(F32),
                                        ALU.subtract).then_inc(base_w_lo_ready, 1)
            top_two(0)
            gating(0)
            dve.wait_ge(lb_hi_ready, 1)
            nc.vector.tensor_tensor(lb_lo[0:EK], lb[0:EK], lb_hi[0:EK].bitcast(F32), ALU.subtract
                                    ).then_inc(lb_lo_ready, 1)
            mixed_lo(1)

            def pair(half):
                for odd in (0, 1):
                    g = 2 * half + 1 + odd
                    turned_lo(g - 1)
                    top_two(g)
                    gating(g)
                    mixed_lo(g + 1)
                    finish(half, odd)

            pair(0)
            with dve.Fori(1, PAIRS) as half:
                pair(half)
            turned_lo(GROUPS - 2)
            top_two(GROUPS - 1)
            gating(GROUPS - 1)
            turned_lo(GROUPS - 1)
            finish(GROUPS // 2 - 1, 0)
            finish(GROUPS // 2 - 1, 1)

        @block.tensor
        def _(pe):
            def three(dst, hi, lo, w_hi, w_lo, start, stop):
                nc.tensor.matmul(dst, hi, w_hi, start=start, stop=False)
                nc.tensor.matmul(dst, hi, w_lo, start=False, stop=False)
                return nc.tensor.matmul(dst, lo, w_hi, start=False, stop=stop)

            def mix(g):
                pe.wait_ge(xw_hi_ready, g + 1)
                pe.wait_ge(xw_lo_ready, g + 1)
                if not isinstance(g, int) or g > 0:
                    pe.wait_ge(y_hi_ready, g)
                    pe.wait_ge(y_lo_ready, g)
                for k in range(TC):
                    last = three(yT_ps[:, k, :], xw_hi[:, k * P:(k + 1) * P], xw_lo[:, k * P:(k + 1) * P],
                                 xw_hi[:, T:XW], xw_lo[:, T:XW], start=True, stop=True)
                last.then_inc(mixed, 1)

            def project(g):
                if isinstance(g, int) and g == 0:
                    pe.wait_ge(hl_w_hi_ready, 1)
                    pe.wait_ge(hl_w_lo_ready, 1)
                pe.wait_ge(y_hi_ready, g + 1)
                if not isinstance(g, int) or g > 0:
                    pe.wait_ge(gated_ready, g)
                for k in range(TC):
                    nc.tensor.matmul(hl_ps[:, 0:HL], y_hi[:, k, :], hl_w_hi[:, k, :], start=(k == 0), stop=False)
                    nc.tensor.matmul(hl_ps[:, 0:HL], y_hi[:, k, :], hl_w_lo[:, k, :], start=False, stop=False)
                pe.wait_ge(y_lo_ready, g + 1)
                for k in range(TC):
                    last = nc.tensor.matmul(hl_ps[:, 0:HL], y_lo[:, k, :], hl_w_hi[:, k, :], start=False,
                                            stop=(k == TC - 1))
                last.then_inc(hl_done, 1)

            def base(g, bank, k0, k1):
                if k0 == 0 and (not isinstance(g, int) or g > 1):
                    pe.wait_ge(result_ready, g - 1)
                for k in range(k0, k1):
                    if isinstance(g, int) and g == 0:
                        pe.wait_ge(base_w_hi_ready, k + 1)
                        pe.wait_ge(base_w_lo_ready, k + 1)
                    three(out_ps[bank][:], y_hi[:, k, :], y_lo[:, k, :], base_w_hi[:, k, :], base_w_lo[:, k, :],
                          start=(k == 0), stop=False)

            def turn(g):
                if isinstance(g, int) and g == 0:
                    pe.wait_ge(ident_ready, 1)
                pe.wait_ge(gated_ready, g + 1)
                if not isinstance(g, int) or g > 0:
                    pe.wait_ge(gT_hi_ready, g)
                    pe.wait_ge(gT_lo_ready, g)
                for h in range(EC):
                    last = nc.tensor.transpose(gT_ps[0:EK, h, 0:P], gated[:, h * EK:(h + 1) * EK], ident[:])
                last.then_inc(turned, 1)

            def lora(g, bank):
                if isinstance(g, int) and g == 0:
                    pe.wait_ge(lb_hi_ready, 1)
                    pe.wait_ge(lb_lo_ready, 1)
                pe.wait_ge(gT_hi_ready, g + 1)
                pe.wait_ge(gT_lo_ready, g + 1)
                for h in range(EC):
                    last = three(out_ps[bank][:], gT_hi[0:EK, h, :], gT_lo[0:EK, h, :], lb_hi[0:EK, h, :],
                                 lb_lo[0:EK, h, :], start=False, stop=(h == EC - 1))
                last.then_inc(out_done, 1)

            mix(0)
            project(0)
            base(0, 0, 0, TC)
            mix(1)

            def pair(half):
                for odd in (0, 1):
                    g = 2 * half + 1 + odd
                    turn(g - 1)
                    project(g)
                    base(g, 1 - odd, 0, TC)
                    mix(g + 1)
                    lora(g - 1, odd)

            pair(0)
            with pe.Fori(1, PAIRS) as half:
                pair(half)
            last_g = GROUPS - 1
            turn(last_g - 1)
            project(last_g)
            base(last_g, 1, 0, TC // 2)
            lora(last_g - 1, 0)
            turn(last_g)
            base(last_g, 1, TC // 2, TC)
            lora(last_g, 1)


def kernel(x, itok_B_0_15, L0_cond_weights, L0_ffn_base_W, L0_ffn_gate_W, L0_ffn_lora_A, L0_ffn_lora_B):
    import numpy as np
    import concourse.bacc as bacc
    from concourse.bass_utils import run_bass_kernel_spmd

    B, C, T = x.shape
    E, R, _ = L0_ffn_lora_A.shape
    D_OUT = L0_ffn_base_W.shape[0]
    lora_aT = np.asarray(L0_ffn_lora_A).reshape(E * R, T).T
    arrays = {
        "x": np.ascontiguousarray(np.asarray(x).reshape(B * C, T)),
        "condition": np.ascontiguousarray(itok_B_0_15),
        "mix_weights": np.ascontiguousarray(L0_cond_weights),
        "base_wT": np.ascontiguousarray(np.asarray(L0_ffn_base_W).T),
        "hl_wT": np.ascontiguousarray(np.concatenate([lora_aT, np.asarray(L0_ffn_gate_W).T], axis=1)),
        "lora_b": np.ascontiguousarray(np.asarray(L0_ffn_lora_B).transpose(0, 2, 1).reshape(E * R, D_OUT)),
    }
    nc = bacc.Bacc("TRN2", target_bir_lowering=False, num_devices=1)
    args = [nc.dram_tensor(name, a.shape, mybir.dt.from_np(a.dtype), kind="ExternalInput").ap()
            for name, a in arrays.items()]
    out = nc.dram_tensor("out", (B * C, D_OUT), F32, kind="ExternalOutput").ap()
    mixed_lora_ffn(nc, *args, out)
    r = run_bass_kernel_spmd(nc, [arrays], core_ids=[0])
    return r.results[0]["out"].reshape(B, C, D_OUT)
```

```python
from contextlib import ExitStack

import concourse.bass as bass
from concourse import mybir

F32 = mybir.dt.float32
F32R = mybir.dt.float32r
I32 = mybir.dt.int32
U32 = mybir.dt.uint32
ALU = mybir.AluOpType
ACT = mybir.ActivationFunctionType

P = 128
TOP8 = 8
SCALING = 16 / 8
AHEAD = 4


def mixed_lora_ffn(nc, x, row_condition, mix_weights, base_wT, hl_wT, lora_b, out):
    ROWS, T = x.shape
    C = mix_weights.shape[1]
    ER, D_OUT = lora_b.shape
    E = hl_wT.shape[1] - ER
    RANK = ER // E
    HL = ER + E
    BATCHES = P // C
    GROUPS = ROWS // P
    TC = T // P
    EC = 2
    EK = ER // EC
    assert GROUPS % 2 == 0 and T % P == 0 and EK <= P and HL <= 512 and D_OUT <= 512

    x_g = x.rearrange("(g p) t -> g p t", p=P)
    out_g = out.rearrange("(g p) t -> g p t", p=P)
    mix_rows = mix_weights.rearrange("n c d -> (n c) d")
    base_v = base_wT.rearrange("(k p) n -> p k n", p=P)
    hl_v = hl_wT.rearrange("(k p) n -> p k n", p=P)
    lora_b_v = lora_b.rearrange("(k p) n -> p k n", p=EK)

    with ExitStack() as ctx:
        def sb(name, shape, dt=F32):
            return ctx.enter_context(nc.sbuf_tensor(name, shape, dt))

        def ps(name, shape):
            return ctx.enter_context(nc.psum_tensor(name, shape, F32))

        def sem(name):
            return ctx.enter_context(nc.semaphore(name))

        x_all = sb("x_all", [P, GROUPS, T])
        mix_all = sb("mix_all", [P, GROUPS, C])
        x_now = sb("x_now", [P, T])
        blocks = sb("blocks", [P, P])
        row_cond = sb("row_cond", [P, GROUPS], I32)
        row = sb("row", [P, GROUPS], I32)
        channel = sb("channel", [P, GROUPS], I32)
        mix_row = sb("mix_row", [P, GROUPS], U32)
        y_hi = sb("y_hi", [P, TC, P], F32R)
        y_lo = sb("y_lo", [P, TC, P], F32R)
        hl_w = sb("hl_w", [P, TC, HL])
        hl_w_hi = sb("hl_w_hi", [P, TC, HL], F32R)
        hl_w_lo = sb("hl_w_lo", [P, TC, HL], F32R)
        base_w = sb("base_w", [P, TC, D_OUT])
        base_w_hi = sb("base_w_hi", [P, TC, D_OUT], F32R)
        base_w_lo = sb("base_w_lo", [P, TC, D_OUT], F32R)
        lb = sb("lb", [P, EC, D_OUT])
        lb_hi = sb("lb_hi", [P, EC, D_OUT], F32R)
        lb_lo = sb("lb_lo", [P, EC, D_OUT], F32R)
        gated = sb("gated", [P, ER])
        gT_hi = sb("gT_hi", [P, EC, P], F32R)
        gT_lo = sb("gT_lo", [P, EC, P], F32R)
        ident = sb("ident", [P, P])
        expert_i = sb("expert_i", [P, E], I32)
        expert = sb("expert", [P, E])
        logit = sb("logit", [P, E])
        top = sb("top", [P, TOP8])
        top_at = sb("top_at", [P, TOP8], U32)
        top_atf = sb("top_atf", [P, 2])
        ratio = sb("ratio", [P, 1])
        halfsum = sb("halfsum", [P, 1])
        norm = sb("norm", [P, 1])
        second = sb("second", [P, E])
        gate = sb("gate", [P, E])
        result = sb("result", [P, 2, D_OUT])

        yT_ps = ps("yT_ps", [P, TC, P])
        hl_ps = ps("hl_ps", [P, 512])
        gT_ps = ps("gT_ps", [P, EC, 256])
        out_ps = [ps(f"out_ps{i}", [P, D_OUT]) for i in range(2)]

        h_ps = hl_ps[:, 0:ER].rearrange("p (e r) -> p e r", r=RANK)

        blocks_zeroed = sem("blocks_zeroed")
        x_loaded = [sem(f"x_loaded{i}") for i in range(2)]
        row_cond_loaded = sem("row_cond_loaded")
        row_ready = sem("row_ready")
        channel_ready = sem("channel_ready")
        mix_row_ready = sem("mix_row_ready")
        mix_gathered = [sem(f"mix_gathered{i}") for i in range(2)]
        hl_w_loaded = sem("hl_w_loaded")
        base_w_loaded = [sem(f"base_w_loaded{k}") for k in range(TC)]
        lb_loaded = sem("lb_loaded")
        hl_w_hi_ready = sem("hl_w_hi_ready")
        hl_w_lo_ready = sem("hl_w_lo_ready")
        base_w_hi_ready = sem("base_w_hi_ready")
        base_w_lo_ready = sem("base_w_lo_ready")
        lb_hi_ready = sem("lb_hi_ready")
        lb_lo_ready = sem("lb_lo_ready")
        ident_zeroed = sem("ident_zeroed")
        ident_ready = sem("ident_ready")
        expert_i_ready = sem("expert_i_ready")
        expert_ready = sem("expert_ready")
        x_staged = sem("x_staged")
        blocks_placed = sem("blocks_placed")
        mixed = sem("mixed")
        y_hi_ready = sem("y_hi_ready")
        y_lo_ready = sem("y_lo_ready")
        hl_done = sem("hl_done")
        logit_ready = sem("logit_ready")
        top_ready = sem("top_ready")
        top_at_ready = sem("top_at_ready")
        top_atf_ready = sem("top_atf_ready")
        ratio_ready = sem("ratio_ready")
        halfsum_ready = sem("halfsum_ready")
        norm_ready = sem("norm_ready")
        second_ready = sem("second_ready")
        gate_ready = sem("gate_ready")
        gated_ready = sem("gated_ready")
        turned = sem("turned")
        gT_hi_ready = sem("gT_hi_ready")
        gT_lo_ready = sem("gT_lo_ready")
        out_done = sem("out_done")
        result_ready = sem("result_ready")
        stored = [sem(f"stored{i}") for i in range(2)]

        PAIRS = (GROUPS - 2) // 2

        block = ctx.enter_context(nc.Block())

        @block.sync
        def _(sp):
            def load(half, odd):
                g = 2 * half + odd
                if not isinstance(half, int) or half > 0:
                    sp.wait_ge(x_loaded[odd], 16 * half)
                sp.dma_start(x_all[:, bass.ds(g, 1), :].rearrange("p a t -> p (a t)"),
                             x_g[bass.ds(g, 1)].rearrange("a p t -> (a p) t")).then_inc(x_loaded[odd], 16)

            def store(half, odd):
                g = 2 * half + odd
                sp.wait_ge(result_ready, g + 1)
                sp.dma_start(out_g[bass.ds(g, 1)].rearrange("a p t -> (a p) t"),
                             result[:, odd, :]).then_inc(stored[odd], 16)

            sp.dma_start(row_cond[:], row_condition).then_inc(row_cond_loaded, 16)
            for g in range(AHEAD):
                load(g // 2, g % 2)
            with sp.Fori(0, (GROUPS - AHEAD) // 2) as half:
                load(half + AHEAD // 2, 0)
                store(half, 0)
                load(half + AHEAD // 2, 1)
                store(half, 1)
            for g in range(GROUPS - AHEAD, GROUPS):
                store(g // 2, g % 2)
            for odd in range(2):
                sp.wait_ge(stored[odd], 16 * (GROUPS // 2))

        @block.gpsimd
        def _(pool):
            nc.gpsimd.iota(row[:], pattern=[[0, GROUPS]], base=0, channel_multiplier=1).then_inc(row_ready, 1)
            nc.gpsimd.iota(expert_i[:], pattern=[[1, E]], base=0, channel_multiplier=0).then_inc(expert_i_ready, 1)
            nc.gpsimd.memset(ident[:], 0.0).then_inc(ident_zeroed, 1)
            pool.wait_ge(mix_row_ready, 1)

            for g in range(GROUPS):
                if g >= 2:
                    pool.wait_ge(mix_gathered[g % 2], 16 * (g // 2))
                nc.gpsimd.indirect_dma_start(
                    out=mix_all[:, g, :], out_offset=None, in_=mix_rows,
                    in_offset=bass.IndirectOffsetOnAxis(ap=mix_row[:, g:g + 1], axis=0),
                ).then_inc(mix_gathered[g % 2], 16)
                if g == 1:
                    pool.wait_ge(ident_zeroed, 1)
                    nc.gpsimd.affine_select(out=ident[:], in_=ident[:], compare_op=ALU.not_equal, fill=1.0,
                                            base=0, pattern=[[-1, P]], channel_multiplier=1
                                            ).then_inc(ident_ready, 1)
                    pool.wait_ge(expert_i_ready, 1)
                    nc.gpsimd.tensor_copy(expert[:], expert_i[:]).then_inc(expert_ready, 1)

        @block.scalar
        def _(act):
            act.dma_start(hl_w[:], hl_v).then_inc(hl_w_loaded, 16)
            for k in range(TC):
                act.dma_start(base_w[:, k, :], base_v[:, k, :]).then_inc(base_w_loaded[k], 16)
            act.dma_start(lb[0:EK], lora_b_v).then_inc(lb_loaded, 16)

            def stage(half, odd):
                g = 2 * half + odd
                act.wait_ge(x_loaded[odd], 16 * (half + 1))
                if not isinstance(g, int) or g > 0:
                    act.wait_ge(mixed, g)
                nc.scalar.copy(x_now[:], x_all[:, bass.ds(g, 1), :].rearrange("p a t -> p (a t)")
                               ).then_inc(x_staged, 1)
                act.wait_ge(mix_gathered[odd], 16 * (half + 1))
                if isinstance(g, int) and g == 0:
                    act.wait_ge(blocks_zeroed, 1)
                for b in range(BATCHES):
                    last = nc.scalar.copy(
                        blocks[b * C:(b + 1) * C, b * C:(b + 1) * C],
                        mix_all[b * C:(b + 1) * C, bass.ds(g, 1), :].rearrange("p a d -> p (a d)"))
                last.then_inc(blocks_placed, 1)

            def mixed_hi(g):
                act.wait_ge(mixed, g + 1)
                if not isinstance(g, int) or g > 0:
                    act.wait_ge(y_lo_ready, g)
                nc.scalar.copy(y_hi[:], yT_ps[:]).then_inc(y_hi_ready, 1)

            def gate_ratio(g):
                act.wait_ge(top_ready, g + 1)
                if not isinstance(g, int) or g > 0:
                    act.wait_ge(gate_ready, g)
                    act.wait_ge(halfsum_ready, g)
                nc.scalar.activation(ratio[:], top[:, 0:1], ACT.Exp, bias=top[:, 1:2], scale=-1.0
                                     ).then_inc(ratio_ready, 1)
                act.wait_ge(top_at_ready, g + 1)
                nc.scalar.copy(top_atf[:], top_at[:, 0:2]).then_inc(top_atf_ready, 1)

            def turned_hi(g):
                act.wait_ge(turned, g + 1)
                if not isinstance(g, int) or g > 0:
                    act.wait_ge(out_done, g)
                    act.wait_ge(gT_lo_ready, g)
                nc.scalar.copy(gT_hi[0:EK], gT_ps[0:EK, :, 0:P]).then_inc(gT_hi_ready, 1)

            stage(0, 0)
            act.wait_ge(hl_w_loaded, 16)
            nc.scalar.copy(hl_w_hi[:], hl_w[:]).then_inc(hl_w_hi_ready, 1)
            mixed_hi(0)
            for k in range(TC):
                act.wait_ge(base_w_loaded[k], 16)
                nc.scalar.copy(base_w_hi[:, k, :], base_w[:, k, :]).then_inc(base_w_hi_ready, 1)
            stage(0, 1)
            gate_ratio(0)
            act.wait_ge(lb_loaded, 16)
            nc.scalar.copy(lb_hi[0:EK], lb[0:EK]).then_inc(lb_hi_ready, 1)
            mixed_hi(1)

            def pair(half):
                for odd in (0, 1):
                    g = 2 * half + 1 + odd
                    turned_hi(g - 1)
                    stage(half + 1, odd)
                    gate_ratio(g)
                    mixed_hi(g + 1)

            pair(0)
            with act.Fori(1, PAIRS) as half:
                pair(half)
            turned_hi(GROUPS - 2)
            gate_ratio(GROUPS - 1)
            turned_hi(GROUPS - 1)

        @block.vector
        def _(dve):
            nc.vector.memset(blocks[:], 0.0).then_inc(blocks_zeroed, 1)
            dve.wait_ge(row_ready, 1)
            nc.vector.tensor_single_scalar(channel[:], row[:], C - 1, ALU.bitwise_and).then_inc(channel_ready, 1)
            dve.wait_ge(channel_ready, 1)
            dve.wait_ge(row_cond_loaded, 16)
            nc.vector.scalar_tensor_tensor(mix_row[:], row_cond[:], float(C), channel[:], ALU.mult, ALU.add
                                           ).then_inc(mix_row_ready, 1)

            def mixed_lo(g):
                dve.wait_ge(y_hi_ready, g + 1)
                nc.vector.tensor_tensor(y_lo[:], yT_ps[:], y_hi[:].bitcast(F32), ALU.subtract
                                        ).then_inc(y_lo_ready, 1)

            def top_two(g):
                dve.wait_ge(hl_done, g + 1)
                nc.vector.tensor_copy(logit[:], hl_ps[:, ER:HL]).then_inc(logit_ready, 1)
                dve.wait_ge(expert_ready, 1)
                dve.wait_ge(logit_ready, g + 1)
                if not isinstance(g, int) or g > 0:
                    dve.wait_ge(ratio_ready, g)
                nc.vector.max(top[:], logit[:]).then_inc(top_ready, 1)
                dve.wait_ge(expert_ready, 1)
                dve.wait_ge(top_ready, g + 1)
                if not isinstance(g, int) or g > 0:
                    dve.wait_ge(top_atf_ready, g)
                nc.vector.max_index(top_at[:], top[:], logit[:]).then_inc(top_at_ready, 1)

            def gating(g):
                dve.wait_ge(ratio_ready, g + 1)
                nc.vector.tensor_scalar(halfsum[:], ratio[:], 1.0, 1.0 / SCALING, ALU.add, ALU.mult
                                        ).then_inc(halfsum_ready, 1)
                dve.wait_ge(top_atf_ready, g + 1)
                nc.vector.tensor_scalar(second[:], expert[:], top_atf[:, 1:2], ratio[:], ALU.is_equal, ALU.mult
                                        ).then_inc(second_ready, 1)
                dve.wait_ge(halfsum_ready, g + 1)
                nc.vector.reciprocal(norm[:], halfsum[:]).then_inc(norm_ready, 1)
                dve.wait_ge(second_ready, g + 1)
                nc.vector.scalar_tensor_tensor(gate[:], expert[:], top_atf[:, 0:1], second[:],
                                               ALU.is_equal, ALU.add).then_inc(gate_ready, 1)
                dve.wait_ge(norm_ready, g + 1)
                dve.wait_ge(gate_ready, g + 1)
                if not isinstance(g, int) or g > 0:
                    dve.wait_ge(turned, g)
                nc.vector.scalar_tensor_tensor(gated[:].rearrange("p (e r) -> p e r", r=RANK), h_ps, norm[:, 0:1],
                                               gate[:].unsqueeze(2).broadcast_to([P, E, RANK]),
                                               ALU.mult, ALU.mult).then_inc(gated_ready, 1)

            def turned_lo(g):
                dve.wait_ge(gT_hi_ready, g + 1)
                if not isinstance(g, int) or g > 0:
                    dve.wait_ge(out_done, g)
                nc.vector.tensor_tensor(gT_lo[0:EK], gT_ps[0:EK, :, 0:P], gT_hi[0:EK].bitcast(F32), ALU.subtract
                                        ).then_inc(gT_lo_ready, 1)

            def finish(half, odd):
                g = 2 * half + odd
                dve.wait_ge(out_done, g + 1)
                if not isinstance(half, int) or half > 0:
                    dve.wait_ge(stored[odd], 16 * half)
                nc.vector.tensor_tensor(result[:, odd, :], out_ps[odd][:],
                                        x_all[:, bass.ds(g, 1), :].rearrange("p a t -> p (a t)"), ALU.add
                                        ).then_inc(result_ready, 1)

            dve.wait_ge(hl_w_hi_ready, 1)
            nc.vector.tensor_tensor(hl_w_lo[:], hl_w[:], hl_w_hi[:].bitcast(F32), ALU.subtract
                                    ).then_inc(hl_w_lo_ready, 1)
            mixed_lo(0)
            for k in range(TC):
                dve.wait_ge(base_w_hi_ready, k + 1)
                nc.vector.tensor_tensor(base_w_lo[:, k, :], base_w[:, k, :], base_w_hi[:, k, :].bitcast(F32),
                                        ALU.subtract).then_inc(base_w_lo_ready, 1)
            top_two(0)
            gating(0)
            dve.wait_ge(lb_hi_ready, 1)
            nc.vector.tensor_tensor(lb_lo[0:EK], lb[0:EK], lb_hi[0:EK].bitcast(F32), ALU.subtract
                                    ).then_inc(lb_lo_ready, 1)
            mixed_lo(1)

            def pair(half):
                for odd in (0, 1):
                    g = 2 * half + 1 + odd
                    turned_lo(g - 1)
                    top_two(g)
                    gating(g)
                    mixed_lo(g + 1)
                    finish(half, odd)

            pair(0)
            with dve.Fori(1, PAIRS) as half:
                pair(half)
            turned_lo(GROUPS - 2)
            top_two(GROUPS - 1)
            gating(GROUPS - 1)
            turned_lo(GROUPS - 1)
            finish(GROUPS // 2 - 1, 0)
            finish(GROUPS // 2 - 1, 1)

        @block.tensor
        def _(pe):
            def three(dst, hi, lo, w_hi, w_lo, start, stop):
                nc.tensor.matmul(dst, hi, w_hi, start=start, stop=False)
                nc.tensor.matmul(dst, hi, w_lo, start=False, stop=False)
                return nc.tensor.matmul(dst, lo, w_hi, start=False, stop=stop)

            def mix(g):
                pe.wait_ge(x_staged, g + 1)
                pe.wait_ge(blocks_placed, g + 1)
                if not isinstance(g, int) or g > 0:
                    pe.wait_ge(y_hi_ready, g)
                    pe.wait_ge(y_lo_ready, g)
                for k in range(TC):
                    last = nc.tensor.matmul(yT_ps[:, k, :], x_now[:, k * P:(k + 1) * P], blocks[:],
                                            start=True, stop=True)
                last.then_inc(mixed, 1)

            def project(g):
                if isinstance(g, int) and g == 0:
                    pe.wait_ge(hl_w_hi_ready, 1)
                    pe.wait_ge(hl_w_lo_ready, 1)
                pe.wait_ge(y_hi_ready, g + 1)
                if not isinstance(g, int) or g > 0:
                    pe.wait_ge(gated_ready, g)
                for k in range(TC):
                    nc.tensor.matmul(hl_ps[:, 0:HL], y_hi[:, k, :], hl_w_hi[:, k, :], start=(k == 0), stop=False)
                    nc.tensor.matmul(hl_ps[:, 0:HL], y_hi[:, k, :], hl_w_lo[:, k, :], start=False, stop=False)
                pe.wait_ge(y_lo_ready, g + 1)
                for k in range(TC):
                    last = nc.tensor.matmul(hl_ps[:, 0:HL], y_lo[:, k, :], hl_w_hi[:, k, :], start=False,
                                            stop=(k == TC - 1))
                last.then_inc(hl_done, 1)

            def base(g, bank, k0, k1):
                if k0 == 0 and (not isinstance(g, int) or g > 1):
                    pe.wait_ge(result_ready, g - 1)
                for k in range(k0, k1):
                    if isinstance(g, int) and g == 0:
                        pe.wait_ge(base_w_hi_ready, k + 1)
                        pe.wait_ge(base_w_lo_ready, k + 1)
                    three(out_ps[bank][:], y_hi[:, k, :], y_lo[:, k, :], base_w_hi[:, k, :], base_w_lo[:, k, :],
                          start=(k == 0), stop=False)

            def turn(g):
                if isinstance(g, int) and g == 0:
                    pe.wait_ge(ident_ready, 1)
                pe.wait_ge(gated_ready, g + 1)
                if not isinstance(g, int) or g > 0:
                    pe.wait_ge(gT_hi_ready, g)
                    pe.wait_ge(gT_lo_ready, g)
                for h in range(EC):
                    last = nc.tensor.transpose(gT_ps[0:EK, h, 0:P], gated[:, h * EK:(h + 1) * EK], ident[:])
                last.then_inc(turned, 1)

            def lora(g, bank):
                if isinstance(g, int) and g == 0:
                    pe.wait_ge(lb_hi_ready, 1)
                    pe.wait_ge(lb_lo_ready, 1)
                pe.wait_ge(gT_hi_ready, g + 1)
                pe.wait_ge(gT_lo_ready, g + 1)
                for h in range(EC):
                    last = three(out_ps[bank][:], gT_hi[0:EK, h, :], gT_lo[0:EK, h, :], lb_hi[0:EK, h, :],
                                 lb_lo[0:EK, h, :], start=False, stop=(h == EC - 1))
                last.then_inc(out_done, 1)

            mix(0)
            project(0)
            base(0, 0, 0, TC)
            mix(1)

            def pair(half):
                for odd in (0, 1):
                    g = 2 * half + 1 + odd
                    turn(g - 1)
                    project(g)
                    base(g, 1 - odd, 0, TC)
                    mix(g + 1)
                    lora(g - 1, odd)

            pair(0)
            with pe.Fori(1, PAIRS) as half:
                pair(half)
            last_g = GROUPS - 1
            turn(last_g - 1)
            project(last_g)
            base(last_g, 1, 0, TC // 2)
            lora(last_g - 1, 0)
            turn(last_g)
            base(last_g, 1, TC // 2, TC)
            lora(last_g, 1)


def kernel(x, itok_B_0_15, L0_cond_weights, L0_ffn_base_W, L0_ffn_gate_W, L0_ffn_lora_A, L0_ffn_lora_B):
    import numpy as np
    import concourse.bacc as bacc
    from concourse.bass_utils import run_bass_kernel_spmd

    B, C, T = x.shape
    E, R, _ = L0_ffn_lora_A.shape
    D_OUT = L0_ffn_base_W.shape[0]
    lora_aT = np.asarray(L0_ffn_lora_A).reshape(E * R, T).T
    arrays = {
        "x": np.ascontiguousarray(np.asarray(x).reshape(B * C, T)),
        "row_condition": np.ascontiguousarray(np.repeat(np.asarray(itok_B_0_15), C).reshape(-1, P).T),
        "mix_weights": np.ascontiguousarray(L0_cond_weights),
        "base_wT": np.ascontiguousarray(np.asarray(L0_ffn_base_W).T),
        "hl_wT": np.ascontiguousarray(np.concatenate([lora_aT, np.asarray(L0_ffn_gate_W).T], axis=1)),
        "lora_b": np.ascontiguousarray(np.asarray(L0_ffn_lora_B).transpose(0, 2, 1).reshape(E * R, D_OUT)),
    }
    nc = bacc.Bacc("TRN2", target_bir_lowering=False, num_devices=1)
    args = [nc.dram_tensor(name, a.shape, mybir.dt.from_np(a.dtype), kind="ExternalInput").ap()
            for name, a in arrays.items()]
    out = nc.dram_tensor("out", (B * C, D_OUT), F32, kind="ExternalOutput").ap()
    mixed_lora_ffn(nc, *args, out)
    r = run_bass_kernel_spmd(nc, [arrays], core_ids=[0])
    return r.results[0]["out"].reshape(B, C, D_OUT)
```

```python
from contextlib import ExitStack

import concourse.bass as bass
from concourse import mybir

F32 = mybir.dt.float32
F32R = mybir.dt.float32r
BF16 = mybir.dt.bfloat16
I32 = mybir.dt.int32
U32 = mybir.dt.uint32
ALU = mybir.AluOpType
ACT = mybir.ActivationFunctionType

P = 128
TOP8 = 8
SCALING = 16 / 8
AHEAD = 4
WARM_UP = 8


def mixed_lora_ffn(nc, x, condition, mix_weights, base_wT, hl_wT, lora_b, out):
    ROWS, T = x.shape
    _, NUM_COND, C = mix_weights.shape
    ER, D_OUT = lora_b.shape
    E = hl_wT.shape[1] - ER
    RANK = ER // E
    HL = ER + E
    BATCHES = P // C
    GROUPS = ROWS // P
    TC = T // P
    EC = 2
    EK = ER // EC
    assert GROUPS % 2 == 0 and T % P == 0 and EK <= P and HL <= 512 and D_OUT <= 512

    x_g = x.rearrange("(g p) t -> g p t", p=P)
    out_g = out.rearrange("(g p) t -> g p t", p=P)
    cond_g = condition.rearrange("(g b) -> g b", b=BATCHES)
    base_v = base_wT.rearrange("(k p) n -> p k n", p=P)
    hl_v = hl_wT.rearrange("(k p) n -> p k n", p=P)
    lora_b_v = lora_b.rearrange("(k p) n -> p k n", p=EK)

    with ExitStack() as ctx:
        def sb(name, shape, dt=F32):
            return ctx.enter_context(nc.sbuf_tensor(name, shape, dt))

        def ps(name, shape):
            return ctx.enter_context(nc.psum_tensor(name, shape, F32))

        def sem(name):
            return ctx.enter_context(nc.semaphore(name))

        x_all = sb("x_all", [P, GROUPS, T])
        mix_w = sb("mix_w", [P, NUM_COND, C])
        x_now = sb("x_now", [P, T])
        blocks = sb("blocks", [P, P])
        y_hi = [sb(f"y_hi{i}", [P, TC, P], F32R) for i in range(2)]
        y_lo = [sb(f"y_lo{i}", [P, TC, P], F32R) for i in range(2)]
        idle = sb("idle", [P, 512], BF16)
        hl_w = sb("hl_w", [P, TC, HL])
        hl_w_hi = sb("hl_w_hi", [P, TC, HL], F32R)
        hl_w_lo = sb("hl_w_lo", [P, TC, HL], F32R)
        base_w = sb("base_w", [P, TC, D_OUT])
        base_w_hi = sb("base_w_hi", [P, TC, D_OUT], F32R)
        base_w_lo = sb("base_w_lo", [P, TC, D_OUT], F32R)
        lb = sb("lb", [P, EC, D_OUT])
        lb_hi = sb("lb_hi", [P, EC, D_OUT], F32R)
        lb_lo = sb("lb_lo", [P, EC, D_OUT], F32R)
        gated = sb("gated", [P, ER])
        gT_hi = sb("gT_hi", [P, EC, P], F32R)
        gT_lo = sb("gT_lo", [P, EC, P], F32R)
        ident = sb("ident", [P, P])
        expert_i = sb("expert_i", [P, E], I32)
        expert = sb("expert", [P, E])
        logit = sb("logit", [P, E])
        top = sb("top", [P, TOP8])
        top_at = sb("top_at", [P, TOP8], U32)
        top_atf = sb("top_atf", [P, 2])
        ratio = sb("ratio", [P, 1])
        halfsum = sb("halfsum", [P, 1])
        norm = sb("norm", [P, 1])
        second = sb("second", [P, E])
        gate = sb("gate", [P, E])
        result = sb("result", [P, 2, D_OUT])

        yT_ps = ps("yT_ps", [P, TC, P])
        hl_ps = ps("hl_ps", [P, 512])
        gT_ps = ps("gT_ps", [P, EC, 256])
        out_ps = [ps(f"out_ps{i}", [P, D_OUT]) for i in range(3)]

        h_ps = hl_ps[:, 0:ER].rearrange("p (e r) -> p e r", r=RANK)

        blocks_zeroed = sem("blocks_zeroed")
        x_loaded = [sem(f"x_loaded{i}") for i in range(2)]
        x_now_loaded = sem("x_now_loaded")
        mix_w_loaded = sem("mix_w_loaded")
        idle_zeroed = sem("idle_zeroed")
        hl_w_loaded = [sem(f"hl_w_loaded{n}") for n in range(2)]
        base_w_loaded = [sem(f"base_w_loaded{k}") for k in range(TC)]
        lb_loaded = sem("lb_loaded")
        hl_w_hi_ready = sem("hl_w_hi_ready")
        hl_w_lo_ready = sem("hl_w_lo_ready")
        base_w_hi_ready = sem("base_w_hi_ready")
        base_w_lo_ready = sem("base_w_lo_ready")
        base_w_last_lo_ready = sem("base_w_last_lo_ready")
        lb_hi_ready = sem("lb_hi_ready")
        lb_lo_ready = sem("lb_lo_ready")
        ident_zeroed = sem("ident_zeroed")
        ident_ready = sem("ident_ready")
        expert_i_ready = sem("expert_i_ready")
        expert_ready = sem("expert_ready")
        x_staged = sem("x_staged")
        blocks_placed = sem("blocks_placed")
        mixed = sem("mixed")
        y_hi_ready = sem("y_hi_ready")
        y_lo_ready = sem("y_lo_ready")
        hl_done = sem("hl_done")
        logit_ready = sem("logit_ready")
        top_ready = sem("top_ready")
        top_at_ready = sem("top_at_ready")
        top_atf_ready = sem("top_atf_ready")
        ratio_ready = sem("ratio_ready")
        halfsum_ready = sem("halfsum_ready")
        norm_ready = sem("norm_ready")
        second_ready = sem("second_ready")
        gate_ready = sem("gate_ready")
        gated_ready = sem("gated_ready")
        turned = sem("turned")
        gT_hi_ready = sem("gT_hi_ready")
        gT_lo_ready = sem("gT_lo_ready")
        out_done = sem("out_done")
        result_ready = sem("result_ready")
        stored = [sem(f"stored{i}") for i in range(2)]

        PAIRS = (GROUPS - 2) // 2

        block = ctx.enter_context(nc.Block())

        @block.sync
        def _(sp):
            def load(half, odd):
                g = 2 * half + odd
                if not isinstance(half, int) or half > 0:
                    sp.wait_ge(x_loaded[odd], 16 * half)
                sp.dma_start(x_all[:, bass.ds(g, 1), :].rearrange("p a t -> p (a t)"),
                             x_g[bass.ds(g, 1)].rearrange("a p t -> (a p) t")).then_inc(x_loaded[odd], 16)

            def store(half, odd):
                g = 2 * half + odd
                sp.wait_ge(result_ready, g + 1)
                sp.dma_start(out_g[bass.ds(g, 1)].rearrange("a p t -> (a p) t"),
                             result[:, odd, :]).then_inc(stored[odd], 16)

            sp.dma_start(mix_w[:], mix_weights).then_inc(mix_w_loaded, 16)
            for n in range(2):
                half_k = slice(n * TC // 2, (n + 1) * TC // 2)
                sp.dma_start(hl_w[:, half_k, :], hl_v[:, half_k, :]).then_inc(hl_w_loaded[n], 16)
            for k in range(TC):
                if k == TC - 1:
                    load(0, 1)
                sp.dma_start(base_w[:, k, :], base_v[:, k, :]).then_inc(base_w_loaded[k], 16)
            sp.dma_start(lb[0:EK], lora_b_v).then_inc(lb_loaded, 16)
            load(0, 0)
            for g in range(2, AHEAD):
                load(g // 2, g % 2)
            with sp.Fori(0, (GROUPS - AHEAD) // 2) as half:
                load(half + AHEAD // 2, 0)
                store(half, 0)
                load(half + AHEAD // 2, 1)
                store(half, 1)
            for g in range(GROUPS - AHEAD, GROUPS - 1):
                store(g // 2, g % 2)
            for n in range(2):
                cols = slice(n * D_OUT // 2, (n + 1) * D_OUT // 2)
                sp.wait_ge(result_ready, GROUPS + n)
                sp.dma_start(out_g[GROUPS - 1][:, cols], result[:, 1, cols]).then_inc(stored[1], 16)
            sp.wait_ge(stored[0], 16 * (GROUPS // 2))
            sp.wait_ge(stored[1], 16 * (GROUPS // 2 + 1))

        @block.gpsimd
        def _(pool):
            pick_regs = [pool.alloc_register(f"pick{b}") for b in range(BATCHES)]

            def place(g):
                pool.load(pick_regs, cond_g[bass.ds(g, 1), :])
                picks = [pool.snap(r, min_val=0, max_val=NUM_COND - 1) for r in pick_regs]
                pool.wait_ge(blocks_zeroed, 1)
                if isinstance(g, int) and g == 0:
                    pool.wait_ge(mix_w_loaded, 16)
                else:
                    pool.wait_ge(mixed, g)
                for b, pick in enumerate(picks):
                    own = slice(b * C, (b + 1) * C)
                    last = nc.gpsimd.tensor_copy(blocks[own, own],
                                                 mix_w[own, bass.ds(pick, 1), :].rearrange("p a d -> p (a d)"))
                last.then_inc(blocks_placed, 1)

            nc.gpsimd.memset(ident[:], 0.0).then_inc(ident_zeroed, 1)
            nc.gpsimd.iota(expert_i[:], pattern=[[1, E]], base=0, channel_multiplier=0).then_inc(expert_i_ready, 1)
            pool.wait_ge(ident_zeroed, 1)
            nc.gpsimd.affine_select(out=ident[:], in_=ident[:], compare_op=ALU.not_equal, fill=1.0, base=0,
                                    pattern=[[-1, P]], channel_multiplier=1).then_inc(ident_ready, 1)
            pool.wait_ge(expert_i_ready, 1)
            nc.gpsimd.tensor_copy(expert[:], expert_i[:]).then_inc(expert_ready, 1)
            pool.wait_ge(ident_ready, 1)
            pool.wait_ge(expert_ready, 1)
            place(0)
            place(1)
            pool.wait_ge(blocks_placed, 2)
            pool.wait_ge(base_w_hi_ready, TC)
            nc.gpsimd.tensor_tensor(base_w_lo[:, TC - 1, :], base_w[:, TC - 1, :],
                                    base_w_hi[:, TC - 1, :].bitcast(F32), ALU.subtract
                                    ).then_inc(base_w_last_lo_ready, 1)
            pool.wait_ge(base_w_last_lo_ready, 1)
            with pool.Fori(2, GROUPS) as g:
                place(g)

        @block.scalar
        def _(act):
            act.dma_start(x_now[:], x_g[0]).then_inc(x_now_loaded, 16)

            def stage(half, odd):
                g = 2 * half + odd
                act.wait_ge(x_loaded[odd], 16 * (half + 1))
                act.wait_ge(mixed, g)
                nc.scalar.copy(x_now[:], x_all[:, bass.ds(g, 1), :].rearrange("p a t -> p (a t)")
                               ).then_inc(x_staged, 1)

            def mixed_hi(g, odd):
                act.wait_ge(mixed, g + 1)
                if not isinstance(g, int) or g > 1:
                    act.wait_ge(y_lo_ready, g - 1)
                nc.scalar.copy(y_hi[odd][:], yT_ps[:]).then_inc(y_hi_ready, 1)

            def gate_ratio(g):
                act.wait_ge(top_ready, g + 1)
                if not isinstance(g, int) or g > 0:
                    act.wait_ge(gate_ready, g)
                    act.wait_ge(halfsum_ready, g)
                nc.scalar.activation(ratio[:], top[:, 0:1], ACT.Exp, bias=top[:, 1:2], scale=-1.0
                                     ).then_inc(ratio_ready, 1)
                act.wait_ge(top_at_ready, g + 1)
                nc.scalar.copy(top_atf[:], top_at[:, 0:2]).then_inc(top_atf_ready, 1)

            def turned_hi(g):
                act.wait_ge(turned, g + 1)
                if not isinstance(g, int) or g > 0:
                    act.wait_ge(out_done, g)
                    act.wait_ge(gT_lo_ready, g)
                nc.scalar.copy(gT_hi[0:EK], gT_ps[0:EK, :, 0:P]).then_inc(gT_hi_ready, 1)

            def hl_w_split(k):
                act.wait_ge(hl_w_loaded[2 * k // TC], 16)
                nc.scalar.copy(hl_w_hi[:, k, :], hl_w[:, k, :]).then_inc(hl_w_hi_ready, 1)

            for k in range(TC):
                hl_w_split(k)
            mixed_hi(0, 0)
            for k in range(TC):
                act.wait_ge(base_w_loaded[k], 16)
                nc.scalar.copy(base_w_hi[:, k, :], base_w[:, k, :]).then_inc(base_w_hi_ready, 1)
            stage(0, 1)
            gate_ratio(0)
            mixed_hi(1, 1)
            act.wait_ge(lb_loaded, 16)
            nc.scalar.copy(lb_hi[0:EK], lb[0:EK]).then_inc(lb_hi_ready, 1)

            def pair(half):
                for odd in (0, 1):
                    g = 2 * half + 1 + odd
                    turned_hi(g - 1)
                    stage(half + 1, odd)
                    gate_ratio(g)
                    mixed_hi(g + 1, odd)

            pair(0)
            with act.Fori(1, PAIRS) as half:
                pair(half)
            turned_hi(GROUPS - 2)
            gate_ratio(GROUPS - 1)
            turned_hi(GROUPS - 1)

        @block.vector
        def _(dve):
            nc.vector.memset(idle[:], 0.0).then_inc(idle_zeroed, 1)
            nc.vector.memset(blocks[:], 0.0).then_inc(blocks_zeroed, 1)

            def mixed_lo(g, odd):
                dve.wait_ge(y_hi_ready, g + 1)
                nc.vector.tensor_tensor(y_lo[odd][:], yT_ps[:], y_hi[odd][:].bitcast(F32), ALU.subtract
                                        ).then_inc(y_lo_ready, 1)

            def top_two(g):
                dve.wait_ge(hl_done, g + 1)
                nc.vector.tensor_copy(logit[:], hl_ps[:, ER:HL]).then_inc(logit_ready, 1)
                dve.wait_ge(expert_ready, 1)
                dve.wait_ge(logit_ready, g + 1)
                if not isinstance(g, int) or g > 0:
                    dve.wait_ge(ratio_ready, g)
                nc.vector.max(top[:], logit[:]).then_inc(top_ready, 1)
                dve.wait_ge(expert_ready, 1)
                dve.wait_ge(top_ready, g + 1)
                if not isinstance(g, int) or g > 0:
                    dve.wait_ge(top_atf_ready, g)
                nc.vector.max_index(top_at[:], top[:], logit[:]).then_inc(top_at_ready, 1)

            def gating(g):
                dve.wait_ge(ratio_ready, g + 1)
                nc.vector.tensor_scalar(halfsum[:], ratio[:], 1.0, 1.0 / SCALING, ALU.add, ALU.mult
                                        ).then_inc(halfsum_ready, 1)
                dve.wait_ge(top_atf_ready, g + 1)
                nc.vector.tensor_scalar(second[:], expert[:], top_atf[:, 1:2], ratio[:], ALU.is_equal, ALU.mult
                                        ).then_inc(second_ready, 1)
                dve.wait_ge(halfsum_ready, g + 1)
                nc.vector.reciprocal(norm[:], halfsum[:]).then_inc(norm_ready, 1)
                dve.wait_ge(second_ready, g + 1)
                nc.vector.scalar_tensor_tensor(gate[:], expert[:], top_atf[:, 0:1], second[:],
                                               ALU.is_equal, ALU.add).then_inc(gate_ready, 1)
                dve.wait_ge(norm_ready, g + 1)
                dve.wait_ge(gate_ready, g + 1)
                if not isinstance(g, int) or g > 0:
                    dve.wait_ge(turned, g)
                nc.vector.scalar_tensor_tensor(gated[:].rearrange("p (e r) -> p e r", r=RANK), h_ps, norm[:, 0:1],
                                               gate[:].unsqueeze(2).broadcast_to([P, E, RANK]),
                                               ALU.mult, ALU.mult).then_inc(gated_ready, 1)

            def turned_lo(g):
                dve.wait_ge(gT_hi_ready, g + 1)
                if not isinstance(g, int) or g > 0:
                    dve.wait_ge(out_done, g)
                nc.vector.tensor_tensor(gT_lo[0:EK], gT_ps[0:EK, :, 0:P], gT_hi[0:EK].bitcast(F32), ALU.subtract
                                        ).then_inc(gT_lo_ready, 1)

            def finish(half, odd):
                g = 2 * half + odd
                dve.wait_ge(out_done, g + 1)
                if not isinstance(half, int) or half > 0:
                    dve.wait_ge(stored[odd], 16 * half)
                nc.vector.tensor_tensor(result[:, odd, :], out_ps[odd][:],
                                        x_all[:, bass.ds(g, 1), :].rearrange("p a t -> p (a t)"), ALU.add
                                        ).then_inc(result_ready, 1)

            def finish_part(n):
                dve.wait_ge(out_done, GROUPS + n)
                if n == 0:
                    dve.wait_ge(stored[1], 16 * (GROUPS // 2 - 1))
                cols = slice(n * D_OUT // 2, (n + 1) * D_OUT // 2)
                nc.vector.tensor_tensor(result[:, 1, cols], out_ps[1 + n][:, cols], x_all[:, GROUPS - 1, cols],
                                        ALU.add).then_inc(result_ready, 1)

            def hl_w_split(k):
                dve.wait_ge(hl_w_hi_ready, k + 1)
                nc.vector.tensor_tensor(hl_w_lo[:, k, :], hl_w[:, k, :], hl_w_hi[:, k, :].bitcast(F32),
                                        ALU.subtract).then_inc(hl_w_lo_ready, 1)

            for k in range(TC):
                hl_w_split(k)
            mixed_lo(0, 0)
            for k in range(TC - 1):
                dve.wait_ge(base_w_hi_ready, k + 1)
                nc.vector.tensor_tensor(base_w_lo[:, k, :], base_w[:, k, :], base_w_hi[:, k, :].bitcast(F32),
                                        ALU.subtract).then_inc(base_w_lo_ready, 1)
            top_two(0)
            gating(0)
            mixed_lo(1, 1)
            dve.wait_ge(lb_hi_ready, 1)
            nc.vector.tensor_tensor(lb_lo[0:EK], lb[0:EK], lb_hi[0:EK].bitcast(F32), ALU.subtract
                                    ).then_inc(lb_lo_ready, 1)

            def pair(half):
                for odd in (0, 1):
                    g = 2 * half + 1 + odd
                    turned_lo(g - 1)
                    top_two(g)
                    gating(g)
                    mixed_lo(g + 1, odd)
                    finish(half, odd)

            pair(0)
            with dve.Fori(1, PAIRS) as half:
                pair(half)
            turned_lo(GROUPS - 2)
            top_two(GROUPS - 1)
            gating(GROUPS - 1)
            turned_lo(GROUPS - 1)
            finish(GROUPS // 2 - 1, 0)
            for n in range(2):
                finish_part(n)

        @block.tensor
        def _(pe):
            def three(dst, hi, lo, w_hi, w_lo, start, stop):
                nc.tensor.matmul(dst, hi, w_hi, start=start, stop=False)
                nc.tensor.matmul(dst, hi, w_lo, start=False, stop=False)
                return nc.tensor.matmul(dst, lo, w_hi, start=False, stop=stop)

            def mix(g):
                if isinstance(g, int) and g == 0:
                    pe.wait_ge(x_now_loaded, 16)
                else:
                    pe.wait_ge(x_staged, g)
                pe.wait_ge(blocks_placed, g + 1)
                if not isinstance(g, int) or g > 0:
                    pe.wait_ge(y_hi_ready, g)
                    pe.wait_ge(y_lo_ready, g)
                for k in range(TC):
                    last = nc.tensor.matmul(yT_ps[:, k, :], x_now[:, k * P:(k + 1) * P], blocks[:],
                                            start=True, stop=True)
                last.then_inc(mixed, 1)

            def project(g, odd):
                pe.wait_ge(y_hi_ready, g + 1)
                if not isinstance(g, int) or g > 0:
                    pe.wait_ge(gated_ready, g)
                for k in range(TC):
                    if isinstance(g, int) and g == 0:
                        pe.wait_ge(hl_w_hi_ready, k + 1)
                    nc.tensor.matmul(hl_ps[:, 0:HL], y_hi[odd][:, k, :], hl_w_hi[:, k, :], start=(k == 0),
                                     stop=False)
                    if isinstance(g, int) and g == 0:
                        pe.wait_ge(hl_w_lo_ready, k + 1)
                    nc.tensor.matmul(hl_ps[:, 0:HL], y_hi[odd][:, k, :], hl_w_lo[:, k, :], start=False, stop=False)
                pe.wait_ge(y_lo_ready, g + 1)
                for k in range(TC):
                    last = nc.tensor.matmul(hl_ps[:, 0:HL], y_lo[odd][:, k, :], hl_w_hi[:, k, :], start=False,
                                            stop=(k == TC - 1))
                last.then_inc(hl_done, 1)

            def base(g, odd, k0, k1, bank=None, cols=slice(0, D_OUT)):
                bank = odd if bank is None else bank
                if k0 == 0 and bank == odd and (not isinstance(g, int) or g > 1):
                    pe.wait_ge(result_ready, g - 1)
                for k in range(k0, k1):
                    if isinstance(g, int) and g == 0:
                        pe.wait_ge(base_w_hi_ready, k + 1)
                        if k < TC - 1:
                            pe.wait_ge(base_w_lo_ready, k + 1)
                        else:
                            pe.wait_ge(base_w_last_lo_ready, 1)
                    three(out_ps[bank][:, cols], y_hi[odd][:, k, :], y_lo[odd][:, k, :], base_w_hi[:, k, cols],
                          base_w_lo[:, k, cols], start=(k == 0), stop=False)

            def turn(g):
                if isinstance(g, int) and g == 0:
                    pe.wait_ge(ident_ready, 1)
                pe.wait_ge(gated_ready, g + 1)
                if not isinstance(g, int) or g > 0:
                    pe.wait_ge(gT_hi_ready, g)
                    pe.wait_ge(gT_lo_ready, g)
                for h in range(EC):
                    last = nc.tensor.transpose(gT_ps[0:EK, h, 0:P], gated[:, h * EK:(h + 1) * EK], ident[:])
                last.then_inc(turned, 1)

            def lora(g, bank, cols=slice(0, D_OUT)):
                if isinstance(g, int) and g == 0:
                    pe.wait_ge(lb_hi_ready, 1)
                    pe.wait_ge(lb_lo_ready, 1)
                pe.wait_ge(gT_hi_ready, g + 1)
                pe.wait_ge(gT_lo_ready, g + 1)
                for h in range(EC):
                    last = three(out_ps[bank][:, cols], gT_hi[0:EK, h, :], gT_lo[0:EK, h, :], lb_hi[0:EK, h, cols],
                                 lb_lo[0:EK, h, cols], start=False, stop=(h == EC - 1))
                last.then_inc(out_done, 1)

            pe.wait_ge(idle_zeroed, 1)
            for _ in range(WARM_UP):
                nc.tensor.matmul(gT_ps[:].rearrange("p a b -> p (a b)"), idle[:, 0:P], idle[:], start=True, stop=True)
            mix(0)
            project(0, 0)
            base(0, 0, 0, TC - 1)
            mix(1)
            base(0, 0, TC - 1, TC)

            def pair(half):
                for odd in (0, 1):
                    g = 2 * half + 1 + odd
                    turn(g - 1)
                    project(g, 1 - odd)
                    base(g, 1 - odd, 0, TC)
                    mix(g + 1)
                    lora(g - 1, odd)

            pair(0)
            with pe.Fori(1, PAIRS) as half:
                pair(half)

            last_g = GROUPS - 1
            left, right = slice(0, D_OUT // 2), slice(D_OUT // 2, D_OUT)
            turn(last_g - 1)
            project(last_g, 1)
            base(last_g, 1, 0, TC, cols=left)
            lora(last_g - 1, 0)
            turn(last_g)
            base(last_g, 1, 0, TC, bank=2, cols=right)
            lora(last_g, 1, left)
            lora(last_g, 2, right)


def kernel(x, itok_B_0_15, L0_cond_weights, L0_ffn_base_W, L0_ffn_gate_W, L0_ffn_lora_A, L0_ffn_lora_B):
    import numpy as np
    import concourse.bacc as bacc
    from concourse.bass_utils import run_bass_kernel_spmd

    B, C, T = x.shape
    E, R, _ = L0_ffn_lora_A.shape
    D_OUT = L0_ffn_base_W.shape[0]
    lora_aT = np.asarray(L0_ffn_lora_A).reshape(E * R, T).T
    arrays = {
        "x": np.ascontiguousarray(np.asarray(x).reshape(B * C, T)),
        "condition": np.ascontiguousarray(itok_B_0_15),
        "mix_weights": np.tile(np.asarray(L0_cond_weights).transpose(1, 0, 2), (P // C, 1, 1)),
        "base_wT": np.ascontiguousarray(np.asarray(L0_ffn_base_W).T),
        "hl_wT": np.ascontiguousarray(np.concatenate([lora_aT, np.asarray(L0_ffn_gate_W).T], axis=1)),
        "lora_b": np.ascontiguousarray(np.asarray(L0_ffn_lora_B).transpose(0, 2, 1).reshape(E * R, D_OUT)),
    }
    nc = bacc.Bacc("TRN2", target_bir_lowering=False, num_devices=1)
    args = [nc.dram_tensor(name, a.shape, mybir.dt.from_np(a.dtype), kind="ExternalInput").ap()
            for name, a in arrays.items()]
    out = nc.dram_tensor("out", (B * C, D_OUT), F32, kind="ExternalOutput").ap()
    mixed_lora_ffn(nc, *args, out)
    r = run_bass_kernel_spmd(nc, [arrays], core_ids=[0])
    return r.results[0]["out"].reshape(B, C, D_OUT)
```
